# Optimizing a Trainium2 kernel written in Bass

```python
import numpy as np
import jax
import jax.numpy as jnp

def _softmax(x, axis=-1):
    return jax.nn.softmax(x, axis=axis)

def _gelu(x):
    return jax.nn.gelu(x, approximate=True)

def _silu(x):
    return jax.nn.silu(x)

def _sigmoid(x):
    return jax.nn.sigmoid(x)

def _layernorm(x, axis=-1, eps=1e-05):
    m = jnp.mean(x, axis=axis, keepdims=True)
    v = jnp.var(x, axis=axis, keepdims=True)
    return (x - m) / jnp.sqrt(v + eps)

def _scatter_add(tgt, idx, src, axis=0):
    return tgt.at[idx].add(src)

def _segment_sum(src, seg, n):
    return jax.ops.segment_sum(src, seg, n)
kernel_name = 'mk_rec_standalone_d1_rec_r8_76b491'

def setup_inputs(seed: int=0):
    np.random.seed(seed)
    _w = jnp.asarray

    def _rec_inputs():
        import jax
        import jax.numpy as jnp
        _rk = jax.random.key(seed)
        r_x = -9.80646e-05 + 1.00041 * jax.random.normal(jax.random.fold_in(_rk, 1), (512, 256), jnp.float32)
        return r_x
    r_x = _rec_inputs()

    def _L0_rec_setup():
        import jax, jax.numpy as jnp
        import numpy as np
        N_FEATURES = 256
        K_DIM = 16
        BATCH = 256
        key = jax.random.key(seed)
        k1, k2, k3 = jax.random.split(key, 3)
        x = jax.random.normal(k1, (BATCH, N_FEATURES), dtype=jnp.float32)
        w = jax.random.normal(k2, (N_FEATURES,), dtype=jnp.float32)
        v = jax.random.normal(k3, (N_FEATURES, K_DIM), dtype=jnp.float32)
        return {'x': x, 'w': w, 'v': v}
    _L0_rec_all = _L0_rec_setup()
    _L0_rec_in = {k: v for k, v in _L0_rec_all.items() if k in ('w', 'v')}
    del _L0_rec_all
    return {'r_x': r_x, 'L0_rec_w': _L0_rec_in['w'], 'L0_rec_v': _L0_rec_in['v']}

def reference(r_x, L0_rec_w, L0_rec_v):
    import jax
    import jax.numpy as jnp

    def _L0_rec_ref(x, w, v):
        import jax, jax.numpy as jnp
        import numpy as np
        N_FEATURES = 256
        K_DIM = 16
        BATCH = 256
        linear = w * x
        vv = v @ v.T
        inter = jnp.einsum('bi,bj,ij->bij', x, x, vv)
        B = x.shape[0]
        return jnp.concatenate([linear, inter.reshape(B, -1)], axis=1)
    y = _L0_rec_ref(r_x, L0_rec_w, L0_rec_v)
    return y

_drawn_inputs = setup_inputs


def setup_inputs(seed=0):
    import zlib

    import numpy as np

    out = dict(_drawn_inputs(seed))
    spreads = {}
    factors = {'L0_rec_w': 3.971}
    for name, (base, spread) in spreads.items():
        noise = np.random.default_rng([zlib.crc32(name.encode()), seed]).standard_normal(out[name].shape)
        drawn = base * np.exp(spread * noise) if base else spread * noise
        out[name] = jnp.asarray(drawn.astype(out[name].dtype))
    for name, factor in factors.items():
        out[name] = (out[name] * factor).astype(out[name].dtype)
    return out
```

```python
import concourse.bass as bass
from concourse import mybir
from contextlib import ExitStack


def pairwise_interactions(nc: bass.Bass, x: bass.AP, w: bass.AP, v: bass.AP, out: bass.AP):
    fp32 = mybir.dt.float32
    bf16 = mybir.dt.bfloat16
    ALU = mybir.AluOpType
    ACT = mybir.ActivationFunctionType

    P = 128
    B, F = x.shape
    K = v.shape[1]
    H = F // P
    PARTS = 3
    TERMS = PARTS * PARTS
    QUAD = 32
    STEP = P // QUAD
    UNIT = 2 * STEP
    ROUND = 32
    ROUNDS = B // ROUND
    STEPS = ROUND // STEP
    UNITS = ROUND // UNIT
    PAIRS = UNIT // 2
    LOT = 3
    LOTS = (ROUNDS - 1) // LOT
    SLOTS = 4
    DMA = 16

    linear_out = out[:, 0:F]
    inter_out = out[:, F:F + F * F]

    ctx = ExitStack()
    with ctx:
        def sb(name, shape, dt=fp32):
            return ctx.enter_context(nc.sbuf_tensor(name, shape, dt))

        def sem(name):
            return ctx.enter_context(nc.semaphore(name))

        x_sb = sb("x_sb", [PARTS * ROUND, ROUNDS * F])
        parts = sb("parts", [PARTS * ROUND, ROUNDS * F], bf16)
        rest0 = sb("rest0", [2 * ROUND, F])
        rest = sb("rest", [2 * ROUND, LOT * F])
        w_sb = sb("w_sb", [ROUND, F])
        linear = sb("linear", [ROUND, ROUNDS * F])
        ident = sb("ident", [P, P])
        pick_left = sb("pick_left", [PARTS * ROUND, ROUND, QUAD], bf16)
        pick_right = sb("pick_right", [PARTS * ROUND, ROUND, QUAD], bf16)
        v_sb = sb("v_sb", [P, H, K])
        vT = sb("vT", [K, F])
        vv = sb("vv", [P, H * F])
        sides = sb("sides", [P, UNITS, 2, 2, F], bf16)
        inter = sb("inter", [P, STEPS, STEP, H * F])

        slot = [ctx.enter_context(nc.psum_tensor(f"slot{n}", [P, 2, 2 * F], fp32)) for n in range(SLOTS)]

        def sides_slot(u):
            return slot[5 * u % SLOTS]

        def pair_slot(u, k):
            return slot[(5 * u + 1 + k) % SLOTS]

        v_loaded = sem("v_loaded")
        w_loaded = sem("w_loaded")
        x_first_loaded = sem("x_first_loaded")
        x_rest_loaded = sem("x_rest_loaded")
        zeroed = sem("zeroed")
        ident_ready = sem("ident_ready")
        picks_ready = sem("picks_ready")
        vT_turned = sem("vT_turned")
        vT_ready = sem("vT_ready")
        vv_done = sem("vv_done")
        vv_ready = sem("vv_ready")
        split0 = sem("split0")
        split = sem("split")
        parts0_ready = sem("parts0_ready")
        parts_ready = sem("parts_ready")
        sides_laid = sem("sides_laid")
        sides_ready = sem("sides_ready")
        pair_made = sem("pair_made")
        pair_scaled = sem("pair_scaled")
        step_stored = [sem(f"step_stored{s}") for s in range(STEPS)]
        linear_made = sem("linear_made")
        linear_stored = sem("linear_stored")

        block = ctx.enter_context(nc.Block())

        @block.sync
        def _(sp):
            for a in range(PARTS):
                sp.dma_start(x_sb[a * ROUND:(a + 1) * ROUND, 0:F], x[0:ROUND, :]).then_inc(x_first_loaded, DMA)
            for a in range(PARTS):
                sp.dma_start(x_sb[a * ROUND:(a + 1) * ROUND, F:].rearrange("p (r f) -> p r f", f=F),
                             x[ROUND:B, :].rearrange("(r p) f -> p r f", p=ROUND)).then_inc(x_rest_loaded, DMA)

            with sp.Fori(0, ROUNDS) as r:
                for s in range(STEPS):
                    sp.wait_ge(pair_scaled, r * (2 * STEPS) + (2 * s + 2))
                    sp.dma_start(inter_out[bass.ds(r * ROUND + s * STEP, STEP), :]
                                 .rearrange("b (p f) -> p b f", p=P),
                                 inter[:, s, :, :]).then_inc(step_stored[s], DMA)
            for s in range(STEPS):
                sp.wait_ge(step_stored[s], DMA * ROUNDS)

        @block.gpsimd
        def _(pool):
            pool.memset(ident[:, :], 0.0).then_inc(zeroed, 1)
            pool.memset(pick_left[:, :, :], 0.0).then_inc(zeroed, 1)
            pool.memset(pick_right[:, :, :], 0.0).then_inc(zeroed, 1)
            pool.wait_ge(zeroed, 1)
            pool.affine_select(out=ident[:, :], in_=ident[:, :], compare_op=ALU.not_equal, fill=1.0,
                               base=0, pattern=[[-1, P]], channel_multiplier=1).then_inc(ident_ready, 1)
            pool.wait_ge(zeroed, 3)
            for pick, pattern in ((pick_left, [[-1, ROUND], [-ROUND, PARTS], [0, PARTS]]),
                                  (pick_right, [[-1, ROUND], [0, PARTS], [-ROUND, PARTS]])):
                columns = pick[:, :, 0:TERMS].rearrange("p e (a c) -> p e a c", c=PARTS)
                pool.affine_select(out=columns, in_=columns, compare_op=ALU.not_equal, fill=1.0,
                                   base=0, pattern=pattern, channel_multiplier=1).then_inc(picks_ready, 1)

            pool.wait_ge(w_loaded, DMA)
            pool.wait_ge(x_first_loaded, PARTS * DMA)
            pool.tensor_tensor(linear[:, 0:F], x_sb[0:ROUND, 0:F], w_sb[:, :], ALU.mult).then_inc(linear_made, 1)
            pool.wait_ge(x_rest_loaded, PARTS * DMA)
            for n in range(LOTS):
                now = slice((1 + n * LOT) * F, (1 + (n + 1) * LOT) * F)
                done = 4 * n
                pool.tensor_copy(parts[:, now], x_sb[:, now]).then_inc(split, 1)
                pool.wait_ge(split, done + 1)
                pool.tensor_tensor(rest[:, :], x_sb[0:2 * ROUND, now], parts[0:2 * ROUND, now],
                                   ALU.subtract).then_inc(split, 1)
                pool.wait_ge(split, done + 2)
                pool.tensor_copy(parts[0:2 * ROUND, now], rest[:, :]).then_inc(split, 1)
                pool.wait_ge(split, done + 3)
                pool.tensor_tensor(rest[0:ROUND, :], rest[0:ROUND, :], parts[0:ROUND, now],
                                   ALU.subtract).then_inc(split, 1)
                pool.wait_ge(split, done + 4)
                pool.tensor_copy(parts[0:ROUND, now], rest[0:ROUND, :]).then_inc(parts_ready, LOT)
                pool.tensor_tensor(linear[:, now].rearrange("p (r f) -> p r f", f=F),
                                   x_sb[0:ROUND, now].rearrange("p (r f) -> p r f", f=F),
                                   w_sb[:, :].rearrange("p (a f) -> p a f", a=1).to_broadcast([ROUND, LOT, F]),
                                   ALU.mult).then_inc(linear_made, 1)
            pool.wait_ge(linear_made, 1 + LOTS)
            pool.dma_start(linear_out.rearrange("(r p) f -> p r f", p=ROUND),
                           linear[:, :].rearrange("p (r f) -> p r f", f=F)).then_inc(linear_stored, DMA)
            pool.wait_ge(linear_stored, DMA)

        @block.tensor
        def _(pe):
            def lay_sides(r, u, to):
                for s in range(2):
                    e = (2 * u + s) * STEP
                    for side, pick in enumerate((pick_left, pick_right)):
                        mm = pe.matmul(to[:, s, side * F:(side + 1) * F],
                                       pick[:, e:e + STEP, :].rearrange("p e k -> p (e k)"),
                                       parts[:, bass.ds(r * F, F)], start=True, stop=True)
                mm.then_inc(sides_laid, 1)

            def make_pairs(r, u, first, last):
                for s in range(2):
                    for k in (2 * s, 2 * s + 1):
                        if k == PAIRS - 1:
                            if not last:
                                pe.wait_ge(sides_ready, r * UNITS + (u + 2))
                        elif not first:
                            pe.wait_ge(pair_scaled, (r * UNITS + u) * PAIRS + (k - 2))
                    for t in range(H):
                        for g in range(STEP):
                            rows = sides[g * QUAD:g * QUAD + TERMS, u, s, :, :]
                            mm = pe.matmul(pair_slot(u, 2 * s + g // 2)[:, g % 2, t * F:(t + 1) * F],
                                           rows[:, 0, t::H], rows[:, 1, :], start=True, stop=True)
                            if t == H - 1 and g % 2 == 1:
                                mm.then_inc(pair_made, 1)

            def round_(r, first, last):
                for u in range(UNITS):
                    unit0, unit_last = first and u == 0, last and u == UNITS - 1
                    if not unit_last:
                        if not unit0:
                            pe.wait_ge(pair_scaled, (r * UNITS + u) * PAIRS - 3)
                        if u < UNITS - 1:
                            lay_sides(r, u + 1, sides_slot(u))
                        else:
                            pe.wait_ge(parts_ready, r + 1)
                            lay_sides(r + 1, 0, sides_slot(u))
                    pe.wait_ge(sides_ready, r * UNITS + (u + 1))
                    make_pairs(r, u, unit0, unit_last)

            pe.wait_ge(v_loaded, DMA)
            pe.wait_ge(ident_ready, 1)
            for h in range(H):
                tr = pe.transpose(slot[0][0:K, 0, h * P:(h + 1) * P], v_sb[:, h, :], ident[:, :])
            tr.then_inc(vT_turned, 1)
            pe.wait_ge(vT_ready, 1)
            for t in range(H):
                mm = pe.matmul(slot[1][:, 0, t * F:(t + 1) * F], vT[:, t::H], vT[:, :], start=True, stop=True)
            mm.then_inc(vv_done, 1)

            pe.wait_ge(picks_ready, 2)
            pe.wait_ge(parts0_ready, 1)
            lay_sides(0, 0, slot[3])
            pe.wait_ge(vv_ready, 1)
            round_(0, True, False)
            with pe.Fori(1, ROUNDS - 1) as r:
                round_(r, False, False)
            round_(ROUNDS - 1, False, True)

        @block.scalar
        def _(act):
            act.dma_start(v_sb[:, :, :], v.rearrange("(h p) k -> p h k", p=P)).then_inc(v_loaded, DMA)
            act.dma_start(w_sb[:, :], w.rearrange("(a f) -> a f", a=1).to_broadcast([ROUND, F])).then_inc(w_loaded, DMA)
            act.wait_ge(vT_turned, 1)
            act.activation(vT[:, :], slot[0][0:K, 0, 0:F], ACT.Copy).then_inc(vT_ready, 1)
            act.wait_ge(vv_done, 1)
            act.activation(vv[:, :], slot[1][:, 0, :], ACT.Copy).then_inc(vv_ready, 1)

            def copy_sides(u, frm):
                act.activation(sides[:, u, :, :, :].rearrange("p s a f -> p s (a f)"), frm[:, :, :],
                               ACT.Copy).then_inc(sides_ready, 1)

            def round_(r, first):
                for u in range(UNITS):
                    act.wait_ge(sides_laid, r * UNITS + (u + 1))
                    if not first:
                        act.wait_ge(pair_made, (r * UNITS + (u + 1 - UNITS)) * PAIRS)
                    if first and u == 0:
                        copy_sides(u, slot[3])
                    else:
                        copy_sides(u, sides_slot((u - 1) % UNITS))

            round_(0, True)
            with act.Fori(1, ROUNDS) as r:
                round_(r, False)

        @block.vector
        def _(dve):
            dve.wait_ge(x_first_loaded, PARTS * DMA)
            dve.tensor_copy(parts[:, 0:F], x_sb[:, 0:F]).then_inc(split0, 1)
            dve.wait_ge(split0, 1)
            dve.tensor_tensor(rest0[:, :], x_sb[0:2 * ROUND, 0:F], parts[0:2 * ROUND, 0:F],
                              ALU.subtract).then_inc(split0, 1)
            dve.wait_ge(split0, 2)
            dve.tensor_copy(parts[0:2 * ROUND, 0:F], rest0[:, :]).then_inc(split0, 1)
            dve.wait_ge(split0, 3)
            dve.tensor_tensor(rest0[0:ROUND, :], rest0[0:ROUND, :], parts[0:ROUND, 0:F],
                              ALU.subtract).then_inc(split0, 1)
            dve.wait_ge(split0, 4)
            dve.tensor_copy(parts[0:ROUND, 0:F], rest0[0:ROUND, :]).then_inc(parts0_ready, 1)

            dve.wait_ge(vv_ready, 1)
            vv_twice = vv[:, :].rearrange("p (a f) -> p a f", a=1).to_broadcast([P, 2, H * F])

            def round_(r, first):
                for s in range(STEPS):
                    for k in range(2):
                        dve.wait_ge(pair_made, r * (2 * STEPS) + (2 * s + k + 1))
                        if not first and k == 0:
                            dve.wait_ge(step_stored[s], r * DMA)
                        dve.tensor_tensor(inter[:, s, 2 * k:2 * k + 2, :],
                                          pair_slot(s // 2, 2 * (s % 2) + k)[:, :, :], vv_twice,
                                          ALU.mult).then_inc(pair_scaled, 1)

            round_(0, True)
            with dve.Fori(1, ROUNDS) as r:
                round_(r, False)


_INS = ['r_x', 'L0_rec_w', 'L0_rec_v']


def kernel(**inputs):
    import numpy as _np
    import concourse.bacc as _bacc
    from concourse import mybir as _mybir
    from concourse.bass_utils import run_bass_kernel_spmd as _run

    nc = _bacc.Bacc("TRN2", target_bir_lowering=False, num_devices=1)
    arrays, args = {}, []
    for name in _INS:
        a = _np.ascontiguousarray(inputs[name])
        arrays[f"in_{name}_dram"] = a
        args.append(nc.dram_tensor(f"in_{name}_dram", a.shape, _mybir.dt.from_np(a.dtype), kind="ExternalInput").ap())
    b, f = inputs['r_x'].shape
    args.append(nc.dram_tensor("out_0_dram", (b, f + f * f), _mybir.dt.float32, kind="ExternalOutput").ap())
    pairwise_interactions(nc, *args)
    r = _run(nc, [arrays], core_ids=[0])
    return r.results[0]["out_0_dram"]
```

```python
import concourse.bass as bass
from concourse import mybir
from contextlib import ExitStack


def pairwise_interactions(nc: bass.Bass, x: bass.AP, w: bass.AP, v: bass.AP, out: bass.AP):
    fp32 = mybir.dt.float32
    bf16 = mybir.dt.bfloat16
    ALU = mybir.AluOpType
    ACT = mybir.ActivationFunctionType

    P = 128
    B, F = x.shape
    K = v.shape[1]
    H = F // P
    PARTS = 3
    TERMS = PARTS * PARTS
    QUAD = 32
    STEP = P // QUAD
    UNIT = 2 * STEP
    ROUND = 32
    ROUNDS = B // ROUND
    STEPS = ROUND // STEP
    UNITS = ROUND // UNIT
    PAIRS = UNIT // 2
    EARLY = 4
    LOT = 3
    LOTS = (ROUNDS - 1) // LOT
    SLOTS = 4
    DMA = 16

    linear_out = out[:, 0:F]
    inter_out = out[:, F:F + F * F]

    ctx = ExitStack()
    with ctx:
        def sb(name, shape, dt=fp32):
            return ctx.enter_context(nc.sbuf_tensor(name, shape, dt))

        def sem(name):
            return ctx.enter_context(nc.semaphore(name))

        x_sb = sb("x_sb", [PARTS * ROUND, ROUNDS * F])
        parts = sb("parts", [PARTS * ROUND, ROUNDS * F], bf16)
        rest0 = sb("rest0", [2 * ROUND, F])
        rest = sb("rest", [2 * ROUND, LOT * F])
        w_sb = sb("w_sb", [ROUND, F])
        linear = sb("linear", [ROUND, ROUNDS * F])
        ident = sb("ident", [P, P])
        pick_left = sb("pick_left", [PARTS * ROUND, ROUND, QUAD], bf16)
        pick_right = sb("pick_right", [PARTS * ROUND, ROUND, QUAD], bf16)
        v_sb = sb("v_sb", [P, H, K])
        vT = sb("vT", [K, F])
        vv = sb("vv", [P, H * F])
        sides = sb("sides", [P, UNITS, 2, 2, F], bf16)
        inter = sb("inter", [P, STEPS, STEP, H * F])

        slot = [ctx.enter_context(nc.psum_tensor(f"slot{n}", [P, 2, 2 * F], fp32)) for n in range(SLOTS)]

        def sides_slot(u):
            return slot[5 * u % SLOTS]

        def pair_slot(u, k):
            return slot[(5 * u + 1 + k) % SLOTS]

        v_loaded = sem("v_loaded")
        w_loaded = sem("w_loaded")
        x_first_loaded = sem("x_first_loaded")
        x_rest_loaded = sem("x_rest_loaded")
        ident_zeroed = sem("ident_zeroed")
        picks_zeroed = sem("picks_zeroed")
        ident_ready = sem("ident_ready")
        picks_ready = sem("picks_ready")
        vT_turned = sem("vT_turned")
        vT_ready = sem("vT_ready")
        vv_done = sem("vv_done")
        vv_ready = sem("vv_ready")
        split0 = sem("split0")
        split = sem("split")
        parts0_ready = sem("parts0_ready")
        parts_ready = sem("parts_ready")
        sides0_laid = sem("sides0_laid")
        sides0_ready = sem("sides0_ready")
        sides_laid = sem("sides_laid")
        sides_ready = sem("sides_ready")
        pair_made = sem("pair_made")
        pair_scaled = sem("pair_scaled")
        step_stored = [sem(f"step_stored{s}") for s in range(STEPS)]
        early_stored = sem("early_stored")
        linear_made = sem("linear_made")
        linear_stored = sem("linear_stored")

        def load_x_first(engine, a):
            engine.dma_start(x_sb[a * ROUND:(a + 1) * ROUND, 0:F], x[0:ROUND, :]).then_inc(x_first_loaded, DMA)

        block = ctx.enter_context(nc.Block())

        @block.sync
        def _(sp):
            sp.dma_start(v_sb[:, :, :], v.rearrange("(h p) k -> p h k", p=P)).then_inc(v_loaded, DMA)
            load_x_first(sp, 0)
            for a in range(PARTS):
                sp.dma_start(x_sb[a * ROUND:(a + 1) * ROUND, F:].rearrange("p (r f) -> p r f", f=F),
                             x[ROUND:B, :].rearrange("(r p) f -> p r f", p=ROUND)).then_inc(x_rest_loaded, DMA)

            for s in range(EARLY):
                for k, stored in enumerate((early_stored, step_stored[s])):
                    row = s * STEP + 2 * k
                    sp.wait_ge(pair_scaled, 2 * s + k + 1)
                    sp.dma_start(inter_out[row:row + 2, :].rearrange("b (p f) -> p b f", p=P),
                                 inter[:, s, 2 * k:2 * k + 2, :]).then_inc(stored, DMA)

            def store_step(r, s):
                sp.wait_ge(pair_scaled, r * (2 * STEPS) + (2 * s + 2))
                sp.dma_start(inter_out[bass.ds(r * ROUND + s * STEP, STEP), :]
                             .rearrange("b (p f) -> p b f", p=P),
                             inter[:, s, :, :]).then_inc(step_stored[s], DMA)

            for s in range(EARLY, STEPS):
                store_step(0, s)
            with sp.Fori(1, ROUNDS) as r:
                for s in range(STEPS):
                    store_step(r, s)
            sp.wait_ge(early_stored, EARLY * DMA)
            for s in range(STEPS):
                sp.wait_ge(step_stored[s], DMA * ROUNDS)

        @block.gpsimd
        def _(pool):
            pool.memset(ident[:, :], 0.0).then_inc(ident_zeroed, 1)
            pool.wait_ge(ident_zeroed, 1)
            pool.affine_select(out=ident[:, :], in_=ident[:, :], compare_op=ALU.not_equal, fill=1.0,
                               base=0, pattern=[[-1, P]], channel_multiplier=1).then_inc(ident_ready, 1)
            for n, (pick, pattern) in enumerate(((pick_left, [[-1, ROUND], [-ROUND, PARTS], [0, PARTS]]),
                                                (pick_right, [[-1, ROUND], [0, PARTS], [-ROUND, PARTS]]))):
                pool.wait_ge(picks_zeroed, n + 1)
                columns = pick[:, :, 0:TERMS].rearrange("p e (a c) -> p e a c", c=PARTS)
                pool.affine_select(out=columns, in_=columns, compare_op=ALU.not_equal, fill=1.0,
                                   base=0, pattern=pattern, channel_multiplier=1).then_inc(picks_ready, 1)

            pool.wait_ge(w_loaded, DMA)
            pool.wait_ge(x_first_loaded, PARTS * DMA)
            pool.tensor_tensor(linear[:, 0:F], x_sb[0:ROUND, 0:F], w_sb[:, :], ALU.mult).then_inc(linear_made, 1)
            pool.wait_ge(x_rest_loaded, PARTS * DMA)
            for n in range(LOTS):
                now = slice((1 + n * LOT) * F, (1 + (n + 1) * LOT) * F)
                done = 4 * n
                pool.tensor_copy(parts[:, now], x_sb[:, now]).then_inc(split, 1)
                pool.wait_ge(split, done + 1)
                pool.tensor_tensor(rest[:, :], x_sb[0:2 * ROUND, now], parts[0:2 * ROUND, now],
                                   ALU.subtract).then_inc(split, 1)
                pool.wait_ge(split, done + 2)
                pool.tensor_copy(parts[0:2 * ROUND, now], rest[:, :]).then_inc(split, 1)
                pool.wait_ge(split, done + 3)
                pool.tensor_tensor(rest[0:ROUND, :], rest[0:ROUND, :], parts[0:ROUND, now],
                                   ALU.subtract).then_inc(split, 1)
                pool.wait_ge(split, done + 4)
                pool.tensor_copy(parts[0:ROUND, now], rest[0:ROUND, :]).then_inc(parts_ready, LOT)
                pool.tensor_tensor(linear[:, now].rearrange("p (r f) -> p r f", f=F),
                                   x_sb[0:ROUND, now].rearrange("p (r f) -> p r f", f=F),
                                   w_sb[:, :].rearrange("p (a f) -> p a f", a=1).to_broadcast([ROUND, LOT, F]),
                                   ALU.mult).then_inc(linear_made, 1)
            pool.wait_ge(linear_made, 1 + LOTS)
            pool.dma_start(linear_out.rearrange("(r p) f -> p r f", p=ROUND),
                           linear[:, :].rearrange("p (r f) -> p r f", f=F)).then_inc(linear_stored, DMA)
            pool.wait_ge(linear_stored, DMA)

        @block.tensor
        def _(pe):
            def lay_step(r, u, s, to):
                e = (2 * u + s) * STEP
                for side, pick in enumerate((pick_left, pick_right)):
                    mm = pe.matmul(to[:, s, side * F:(side + 1) * F],
                                   pick[:, e:e + STEP, :].rearrange("p e k -> p (e k)"),
                                   parts[:, bass.ds(r * F, F)], start=True, stop=True)
                return mm

            def lay_unit(r, u, to):
                lay_step(r, u, 0, to)
                lay_step(r, u, 1, to).then_inc(sides_laid, 1)

            def multiply(u, s, g, t):
                rows = sides[g * QUAD:g * QUAD + TERMS, u, s, :, :]
                return pe.matmul(pair_slot(u, 2 * s + g // 2)[:, g % 2, t * F:(t + 1) * F],
                                 rows[:, 0, t::H], rows[:, 1, :], start=True, stop=True)

            def make_unit(r, u, last):
                for s in range(2):
                    for k in (2 * s, 2 * s + 1):
                        if k < PAIRS - 1:
                            pe.wait_ge(pair_scaled, (r * UNITS + u) * PAIRS + (k - 2))
                        elif not last:
                            pe.wait_ge(sides_ready, r * UNITS + (u + 1))
                    for t in range(H):
                        for g in range(STEP):
                            mm = multiply(u, s, g, t)
                            if t == H - 1 and g % 2 == 1:
                                mm.then_inc(pair_made, 1)

            def units(r, us, last=False):
                for u in us:
                    unit_last = last and u == UNITS - 1
                    if not unit_last:
                        pe.wait_ge(pair_scaled, (r * UNITS + u) * PAIRS - 3)
                        if u < UNITS - 1:
                            lay_unit(r, u + 1, sides_slot(u))
                        else:
                            pe.wait_ge(parts_ready, r + 1)
                            lay_unit(r + 1, 0, sides_slot(u))
                    pe.wait_ge(sides_ready, r * UNITS + u)
                    make_unit(r, u, unit_last)

            pe.wait_ge(v_loaded, DMA)
            pe.wait_ge(ident_ready, 1)
            for h in range(H):
                tr = pe.transpose(slot[0][0:K, 0, h * P:(h + 1) * P], v_sb[:, h, :], ident[:, :])
            tr.then_inc(vT_turned, 1)
            pe.wait_ge(vT_ready, 1)
            for t in range(H):
                mm = pe.matmul(slot[1][:, 0, t * F:(t + 1) * F], vT[:, t::H], vT[:, :], start=True, stop=True)
            mm.then_inc(vv_done, 1)

            pe.wait_ge(picks_ready, 2)
            pe.wait_ge(parts0_ready, 1)
            for s in range(2):
                lay_step(0, 0, s, slot[3]).then_inc(sides0_laid, 1)

            for s in range(2):
                pe.wait_ge(sides0_ready, s + 1)
                for k in range(2):
                    if s == 0 and k == 0:
                        pe.wait_ge(vv_ready, 1)
                    if s == 1 and k == 1:
                        pe.wait_ge(sides_ready, 1)
                    for t in range(H):
                        for g in (2 * k, 2 * k + 1):
                            mm = multiply(0, s, g, t)
                    mm.then_inc(pair_made, 1)
                if s == 0:
                    lay_unit(0, 1, sides_slot(0))

            units(0, range(1, UNITS))
            with pe.Fori(1, ROUNDS - 1) as r:
                units(r, range(UNITS))
            units(ROUNDS - 1, range(UNITS), last=True)

        @block.scalar
        def _(act):
            load_x_first(act, 1)
            load_x_first(act, 2)
            act.dma_start(w_sb[:, :], w.rearrange("(a f) -> a f", a=1).to_broadcast([ROUND, F])).then_inc(w_loaded, DMA)
            act.wait_ge(vv_done, 1)
            act.activation(vv[:, :], slot[1][:, 0, :], ACT.Copy).then_inc(vv_ready, 1)

            for s in range(2):
                act.wait_ge(sides0_laid, s + 1)
                act.activation(sides[:, 0, s, :, :].rearrange("p a f -> p (a f)"), slot[3][:, s, :],
                               ACT.Copy).then_inc(sides0_ready, 1)

            def copy_unit(r, u, first):
                act.wait_ge(sides_laid, r * UNITS + u)
                if not first:
                    act.wait_ge(pair_made, (r * UNITS + (u + 1 - UNITS)) * PAIRS)
                act.activation(sides[:, u, :, :, :].rearrange("p s a f -> p s (a f)"),
                               sides_slot((u - 1) % UNITS)[:, :, :], ACT.Copy).then_inc(sides_ready, 1)

            for u in range(1, UNITS):
                copy_unit(0, u, True)
            with act.Fori(1, ROUNDS) as r:
                for u in range(UNITS):
                    copy_unit(r, u, False)

        @block.vector
        def _(dve):
            dve.memset(pick_left[:, :, :], 0.0).then_inc(picks_zeroed, 1)
            dve.memset(pick_right[:, :, :], 0.0).then_inc(picks_zeroed, 1)
            dve.wait_ge(vT_turned, 1)
            dve.tensor_copy(vT[:, :], slot[0][0:K, 0, 0:F]).then_inc(vT_ready, 1)

            dve.wait_ge(x_first_loaded, PARTS * DMA)
            dve.tensor_copy(parts[:, 0:F], x_sb[:, 0:F]).then_inc(split0, 1)
            dve.wait_ge(split0, 1)
            dve.tensor_tensor(rest0[:, :], x_sb[0:2 * ROUND, 0:F], parts[0:2 * ROUND, 0:F],
                              ALU.subtract).then_inc(split0, 1)
            dve.wait_ge(split0, 2)
            dve.tensor_copy(parts[0:2 * ROUND, 0:F], rest0[:, :]).then_inc(split0, 1)
            dve.wait_ge(split0, 3)
            dve.tensor_tensor(rest0[0:ROUND, :], rest0[0:ROUND, :], parts[0:ROUND, 0:F],
                              ALU.subtract).then_inc(split0, 1)
            dve.wait_ge(split0, 4)
            dve.tensor_copy(parts[0:ROUND, 0:F], rest0[0:ROUND, :]).then_inc(parts0_ready, 1)

            dve.wait_ge(vv_ready, 1)
            vv_twice = vv[:, :].rearrange("p (a f) -> p a f", a=1).to_broadcast([P, 2, H * F])

            def round_(r, first):
                for s in range(STEPS):
                    for k in range(2):
                        dve.wait_ge(pair_made, r * (2 * STEPS) + (2 * s + k + 1))
                        if not first and k == 0:
                            dve.wait_ge(step_stored[s], r * DMA)
                        dve.tensor_tensor(inter[:, s, 2 * k:2 * k + 2, :],
                                          pair_slot(s // 2, 2 * (s % 2) + k)[:, :, :], vv_twice,
                                          ALU.mult).then_inc(pair_scaled, 1)

            round_(0, True)
            dve.wait_ge(early_stored, EARLY * DMA)
            with dve.Fori(1, ROUNDS) as r:
                round_(r, False)


_INS = ['r_x', 'L0_rec_w', 'L0_rec_v']


def kernel(**inputs):
    import numpy as _np
    import concourse.bacc as _bacc
    from concourse import mybir as _mybir
    from concourse.bass_utils import run_bass_kernel_spmd as _run

    nc = _bacc.Bacc("TRN2", target_bir_lowering=False, num_devices=1)
    arrays, args = {}, []
    for name in _INS:
        a = _np.ascontiguousarray(inputs[name])
        arrays[f"in_{name}_dram"] = a
        args.append(nc.dram_tensor(f"in_{name}_dram", a.shape, _mybir.dt.from_np(a.dtype), kind="ExternalInput").ap())
    b, f = inputs['r_x'].shape
    args.append(nc.dram_tensor("out_0_dram", (b, f + f * f), _mybir.dt.float32, kind="ExternalOutput").ap())
    pairwise_interactions(nc, *args)
    r = _run(nc, [arrays], core_ids=[0])
    return r.results[0]["out_0_dram"]
```
